# Optimizing a Trainium2 kernel written in Bass

```python
import numpy as np
import jax
import jax.numpy as jnp

def _softmax(x, axis=-1):
    return jax.nn.softmax(x, axis=axis)
def _gelu(x):
    return jax.nn.gelu(x, approximate=True)
def _silu(x):
    return jax.nn.silu(x)
def _sigmoid(x):
    return jax.nn.sigmoid(x)
def _layernorm(x, axis=-1, eps=1e-5):
    m = jnp.mean(x, axis=axis, keepdims=True)
    v = jnp.var(x, axis=axis, keepdims=True)
    return (x - m) / jnp.sqrt(v + eps)
def _scatter_add(tgt, idx, src, axis=0):
    return tgt.at[idx].add(src)
def _segment_sum(src, seg, n):
    return jax.ops.segment_sum(src, seg, n)

kernel_name = 'mk_conv_seq_d2_conv_nchw64_685f7f'

def setup_inputs(seed: int = 0):
    np.random.seed(seed)
    _w = jnp.asarray
    def _rec_inputs():
        import jax
        import jax.numpy as jnp
        _gk = jax.random.key(seed)
        x = -0.0002023 + 1 * jax.random.normal(jax.random.fold_in(_gk, 1), (32, 64, 56, 56), jnp.float32)
        return x
    x = _rec_inputs()
    def _L0_conv_setup():
        import jax, jax.numpy as jnp
        import numpy as np
        G = 8
        CPG = 8
        C = G * CPG
        OC2 = CPG * (CPG + 1) // 2
        OC3 = CPG * (CPG + 1) * (CPG + 2) // 6
        CONV3_SCALE = 0.1
        _I2, _J2 = np.triu_indices(CPG)
        _T3 = np.array([(i, j, k) for i in range(CPG) for j in range(i, CPG) for k in range(j, CPG)], dtype=np.int32)
        _I3, _J3, _K3 = (_T3[:, 0], _T3[:, 1], _T3[:, 2])
        key = jax.random.key(seed)
        ks = jax.random.split(key, 5)
        B, H, W = (32, 56, 56)
        inp = jax.random.normal(ks[0], (B, C, H, W), dtype=jnp.float32)
        W2 = jax.random.normal(ks[1], (G, CPG, OC2), dtype=jnp.float32) * (1.0 / np.sqrt(OC2))
        b2 = jax.random.normal(ks[2], (C,), dtype=jnp.float32) * 0.01
        W3 = jax.random.normal(ks[3], (G, CPG, OC3), dtype=jnp.float32) * (1.0 / np.sqrt(OC3))
        b3 = jax.random.normal(ks[4], (C,), dtype=jnp.float32) * 0.01
        beta2 = jnp.ones((1, C, 1, 1), dtype=jnp.float32)
        beta3 = jnp.ones((1, C, 1, 1), dtype=jnp.float32)
        return {'inp': inp, 'W2': W2, 'b2': b2, 'W3': W3, 'b3': b3, 'beta2': beta2, 'beta3': beta3}
    _L0_conv_all = _L0_conv_setup()
    _L0_conv_in = {k: v for k, v in _L0_conv_all.items() if k in ('W2', 'b2', 'W3', 'b3', 'beta2', 'beta3', )}
    del _L0_conv_all

    def _L1_conv_setup():
        import jax, jax.numpy as jnp
        import numpy as np
        N, C, H, W = (8, 64, 56, 56)
        NL_C = 0.5
        EPS = 1e-05

        def _bn(x, gamma, beta, mean, var):
            inv = jax.lax.rsqrt(var + EPS)
            return (x - mean[:, None, None]) * (inv * gamma)[:, None, None] + beta[:, None, None]
        key = jax.random.key(seed)
        ks = jax.random.split(key, 11)
        l = jax.random.normal(ks[0], (N, C, H, W), jnp.float32)
        w_inside = jax.random.normal(ks[1], (C, C, 1, 1), jnp.float32) * 0.1
        gamma1 = jax.random.normal(ks[2], (C,), jnp.float32)
        beta1 = jax.random.normal(ks[3], (C,), jnp.float32)
        mean1 = jax.random.normal(ks[4], (C,), jnp.float32)
        var1 = jax.random.uniform(ks[5], (C,), jnp.float32, 0.5, 1.5)
        w_dw = jax.random.normal(ks[6], (C, 1, 3, 3), jnp.float32) * 0.1
        gamma2 = jax.random.normal(ks[7], (C,), jnp.float32)
        beta2 = jax.random.normal(ks[8], (C,), jnp.float32)
        mean2 = jax.random.normal(ks[9], (C,), jnp.float32)
        var2 = jax.random.uniform(ks[10], (C,), jnp.float32, 0.5, 1.5)
        return dict(l=l, w_inside=w_inside, gamma1=gamma1, beta1=beta1, mean1=mean1, var1=var1, w_dw=w_dw, gamma2=gamma2, beta2=beta2, mean2=mean2, var2=var2)
    _L1_conv_all = _L1_conv_setup()
    _L1_conv_in = {k: v for k, v in _L1_conv_all.items() if k in ('w_inside', 'gamma1', 'beta1', 'mean1', 'var1', 'w_dw', 'gamma2', 'beta2', 'mean2', 'var2', )}
    del _L1_conv_all

    return {
        "x": x,
        "L0_conv_W2": _L0_conv_in["W2"],
        "L0_conv_b2": _L0_conv_in["b2"],
        "L0_conv_W3": _L0_conv_in["W3"],
        "L0_conv_b3": _L0_conv_in["b3"],
        "L0_conv_beta2": _L0_conv_in["beta2"],
        "L0_conv_beta3": _L0_conv_in["beta3"],
        "L1_conv_w_inside": _L1_conv_in["w_inside"],
        "L1_conv_gamma1": _L1_conv_in["gamma1"],
        "L1_conv_beta1": _L1_conv_in["beta1"],
        "L1_conv_mean1": _L1_conv_in["mean1"],
        "L1_conv_var1": _L1_conv_in["var1"],
        "L1_conv_w_dw": _L1_conv_in["w_dw"],
        "L1_conv_gamma2": _L1_conv_in["gamma2"],
        "L1_conv_beta2": _L1_conv_in["beta2"],
        "L1_conv_mean2": _L1_conv_in["mean2"],
        "L1_conv_var2": _L1_conv_in["var2"],
    }

def reference(x, L0_conv_W2, L0_conv_b2, L0_conv_W3, L0_conv_b3, L0_conv_beta2, L0_conv_beta3, L1_conv_w_inside, L1_conv_gamma1, L1_conv_beta1, L1_conv_mean1, L1_conv_var1, L1_conv_w_dw, L1_conv_gamma2, L1_conv_beta2, L1_conv_mean2, L1_conv_var2):
    import jax
    import jax.numpy as jnp
    def _L0_conv_ref(inp, W2, b2, W3, b3, beta2, beta3):
        import jax, jax.numpy as jnp
        import numpy as np
        G = 8
        CPG = 8
        C = G * CPG
        OC2 = CPG * (CPG + 1) // 2
        OC3 = CPG * (CPG + 1) * (CPG + 2) // 6
        CONV3_SCALE = 0.1
        _I2, _J2 = np.triu_indices(CPG)
        _T3 = np.array([(i, j, k) for i in range(CPG) for j in range(i, CPG) for k in range(j, CPG)], dtype=np.int32)
        _I3, _J3, _K3 = (_T3[:, 0], _T3[:, 1], _T3[:, 2])
        B, Ch, H, Wd = inp.shape
        x = inp.reshape(B, G, CPG, H, Wd)
        p2 = x[:, :, _I2] * x[:, :, _J2]
        y2 = jnp.einsum('bgihw,goi->bgohw', p2, W2).reshape(B, Ch, H, Wd) + b2[None, :, None, None]
        p3 = x[:, :, _I3] * x[:, :, _J3] * x[:, :, _K3]
        y3 = jnp.einsum('bgihw,goi->bgohw', p3, W3).reshape(B, Ch, H, Wd) + b3[None, :, None, None]
        return inp + y2 * beta2 + y3 * beta3 * CONV3_SCALE

    def _L1_conv_ref(l, w_inside, gamma1, beta1, mean1, var1, w_dw, gamma2, beta2, mean2, var2):
        import jax, jax.numpy as jnp
        import numpy as np
        N, C, H, W = (8, 64, 56, 56)
        NL_C = 0.5
        EPS = 1e-05

        def _bn(x, gamma, beta, mean, var):
            inv = jax.lax.rsqrt(var + EPS)
            return (x - mean[:, None, None]) * (inv * gamma)[:, None, None] + beta[:, None, None]
        n, n_in, h, w = l.shape
        c_red = int(NL_C * n_in)
        g = jax.lax.conv_general_dilated(l, w_inside, (1, 1), 'VALID', dimension_numbers=('NCHW', 'OIHW', 'NCHW'))
        g = jnp.clip(_bn(g, gamma1, beta1, mean1, var1), 0.0, 6.0)
        theta = l[:, :c_red]
        f = jnp.einsum('niab,nicd->nabcd', theta, theta)
        f = jax.nn.softmax(f.reshape(n, h * w, h, w), axis=1)
        f = jax.nn.softmax(f.reshape(n, h * w, h * w), axis=2)
        f = f.reshape(n, h, w, h, w)
        out = jnp.einsum('nabcd,nicd->niab', f, g)
        out = out / h * w
        out = jax.lax.conv_general_dilated(out, w_dw, (1, 1), ((1, 1), (1, 1)), dimension_numbers=('NCHW', 'OIHW', 'NCHW'), feature_group_count=n_in)
        out = _bn(out, gamma2, beta2, mean2, var2)
        return out + l

    def _gn(v, G=32, eps=1e-5):
        B_, C_, H_, W_ = v.shape
        g = v.reshape(B_, G, C_ // G, H_, W_)
        m = jnp.mean(g, axis=(2, 3, 4), keepdims=True)
        s = jnp.var(g, axis=(2, 3, 4), keepdims=True)
        return ((g - m) / jnp.sqrt(s + eps)).reshape(v.shape)

    def _ln_c(v, eps=1e-6):
        m = jnp.mean(v, axis=1, keepdims=True)
        s = jnp.var(v, axis=1, keepdims=True)
        return (v - m) / jnp.sqrt(s + eps)

    def _ln_t(v, eps=1e-5):
        m = jnp.mean(v, axis=-1, keepdims=True)
        s = jnp.var(v, axis=-1, keepdims=True)
        return (v - m) / jnp.sqrt(s + eps)

    def _to_tokens(v):
        B_, C_, H_, W_ = v.shape
        return v.reshape(B_, C_, H_ * W_).transpose(0, 2, 1)
    def _from_tokens(t, like):
        B_, C_, H_, W_ = like.shape
        return t.transpose(0, 2, 1).reshape(B_, C_, H_, W_)

    x = _L0_conv_ref(x, L0_conv_W2, L0_conv_b2, L0_conv_W3, L0_conv_b3, L0_conv_beta2, L0_conv_beta3)
    x = _L1_conv_ref(x, L1_conv_w_inside, L1_conv_gamma1, L1_conv_beta1, L1_conv_mean1, L1_conv_var1, L1_conv_w_dw, L1_conv_gamma2, L1_conv_beta2, L1_conv_mean2, L1_conv_var2)
    return x


_drawn_inputs = setup_inputs


def setup_inputs(seed=0):
    import zlib

    import numpy as np

    out = dict(_drawn_inputs(seed))
    spreads = {'L0_conv_beta2': (1.0, 0.2), 'L0_conv_beta3': (1.0, 0.6)}
    factors = {'L0_conv_b2': 8.0,
     'L0_conv_b3': 54.061,
     'L1_conv_var1': 184.369,
     'L1_conv_w_inside': 13.028,
     'L1_conv_mean1': 8.694}
    for name, (base, spread) in spreads.items():
        noise = np.random.default_rng([zlib.crc32(name.encode()), seed]).standard_normal(out[name].shape)
        drawn = base * np.exp(spread * noise) if base else spread * noise
        out[name] = jnp.asarray(drawn.astype(out[name].dtype))
    for name, factor in factors.items():
        out[name] = (out[name] * factor).astype(out[name].dtype)
    return out
```

```python
from contextlib import ExitStack

import numpy as np

import concourse.bass as bass
import concourse.mybir as mybir

F32 = mybir.dt.float32
F32R = mybir.dt.float32r
ALU = mybir.AluOpType
ACT = mybir.ActivationFunctionType
AX = mybir.AxisListType

C, H, W = 64, 56, 56
HW = H * W
G, CPG = 8, 8
EPS = 1e-5

NCH = 7
CH = HW // NCH

NT = 25
KEYS = [128] * 24 + [64]
MAIN = 3072
REM = HW - MAIN
GROUPS = [range(a, b) for a, b in ((0, 4), (4, 8), (8, 12), (12, 16), (16, 19), (19, 22), (22, 25))]
BATCHES = [range(0, 7), range(7, 13), range(13, 19), range(19, 25)]
RING = 10
QC = 392
HALF = 1536


def group_of(t):
    return next(g for g, r in enumerate(GROUPS) if t in r)


def batch_of(t):
    return next(b for b, r in enumerate(BATCHES) if t in r)


class Fill:

    def __init__(self, kind, n, i, j, step):
        self.kind, self.n, self.i, self.j, self.step = kind, n, i, j, step
        if kind in "gr":
            self.ops = [(t, 0) for t in BATCHES[i]]
            self.cost = 115 if kind == "g" else 35
        elif kind == "o":
            self.ops = [(t, h) for t in GROUPS[i] for h in range(2)]
            self.cost = 348
        else:
            self.ops = [(t, q) for t in GROUPS[i] for q in range(4)]
            self.cost = 179


def plan(n_img, budget):
    pre = []
    for n in range(n_img):
        for b, r in enumerate(BATCHES):
            pre.append(Fill("r", n, b, 0, NT * n + r[0] - 3))
            pre.append(Fill("g", n, b, 0, -3 if n == 0 else NT * (n - 1) + 10 + 3 * b))
    pre.sort(key=lambda f: f.step)
    main = []
    for n in range(n_img):
        for g, r in enumerate(GROUPS):
            step = NT * n + r[-1] + 3
            main += [Fill("o", n, g, p, step) for p in range(4)]
            main += [Fill("z", n, g, i, step) for i in range(2)]
    steps, fills, ended = {}, [], {}
    s, cur, at = -3, None, 0
    while pre or main or cur:
        left, todo = budget, []
        while left > 0 or s < 0:
            if cur is None:
                if pre and pre[0].step <= s:
                    cur = pre.pop(0)
                elif main and main[0].step <= s:
                    cur = main.pop(0)
                else:
                    break
                fills.append(cur)
                at = 0
            todo.append((len(fills) - 1, at))
            left -= cur.cost
            at += 1
            if at == len(cur.ops):
                ended[len(fills) - 1] = s
                cur = None
        steps[s] = todo
        s += 1
    return steps, fills, ended, s


def build(nc, a, out, n_img):
    x = a["x"].rearrange("n c h w -> n c (h w)")
    yd = nc.dram_tensor("yd", (n_img, C, HW), F32, kind="Internal").ap()
    hld = nc.dram_tensor("hld", (n_img, 2, 32, HW), F32, kind="Internal").ap()
    layer0(nc, a, x, yd, hld, n_img)
    attention(nc, a, yd, hld, out.rearrange("n c h w -> n c (h w)"), n_img)


def layer0(nc, a, x, yd, hld, n_img):
    ctx = ExitStack()
    with ctx:
        def sb(name, shape, dt=F32):
            return ctx.enter_context(nc.sbuf_tensor("l0_" + name, shape, dt))

        def sem(name):
            return ctx.enter_context(nc.semaphore("l0_" + name))

        X2 = [sb(f"X2{i}", [128, HW]) for i in range(2)]
        X4 = [sb(f"X4{i}", [128, HW]) for i in range(2)]
        YO = [sb(f"YO{i}", [128, HW]) for i in range(2)]
        HO = sb("HO", [64, HW], F32R)
        LO = sb("LO", [64, HW], F32R)
        XX = [sb(f"XX{i}", [128, CH], F32R) for i in range(4)]
        XB = [sb(f"XB{i}", [128, CH]) for i in range(4)]
        P2 = [sb(f"P2{i}", [128, CH]) for i in range(2)]
        U = [sb(f"U{i}", [128, CH]) for i in range(2)]
        self_ = sb("self", [128, 8, 128])
        sel = sb("sel", [128, 8, 128], F32R)
        R = sb("R", [128, 32])
        alpha = sb("alpha", [128, 1])
        W3 = sb("W3", [128, 4, 128])
        W2 = sb("W2", [128, 4, 128])
        be3 = sb("be3", [128, 4, 128])
        be2 = sb("be2", [128, 4, 128])
        bias = sb("bias", [128, 4])
        bt = sb("bt", [128, 3])
        A = [ctx.enter_context(nc.psum_tensor(f"l0_A{i}", [128, 512], F32)) for i in range(2)]
        B = [ctx.enter_context(nc.psum_tensor(f"l0_B{i}", [128, 512], F32)) for i in range(2)]
        T = [ctx.enter_context(nc.psum_tensor(f"l0_T{i}", [128, 512], F32)) for i in range(2)]
        Y = [ctx.enter_context(nc.psum_tensor(f"l0_Y{i}", [128, 512], F32)) for i in range(2)]

        s_c = sem("c")
        s_ld = [sem(f"ld{i}") for i in range(2)]
        s_st = [sem(f"st{i}") for i in range(2)]
        s_ms = sem("ms")
        v_w = sem("vw")
        v_wt = sem("vwt")
        p_ab = sem("pab")
        p_t = sem("pt")
        p_r = sem("pr")
        a_xb = sem("axb")
        a_h = sem("ah")
        a_hy = sem("ahy")
        g_l = sem("gl")
        g_ly = sem("gly")
        v_p2 = sem("vp2")
        v_u = sem("vu")
        v_y = sem("vy")

        NU = NCH * n_img
        NQ = 4 * NU

        def loaded(eng, n):
            eng.wait_ge(s_ld[n % 2], 96 * (n // 2 + 1))

        def stored(eng, n):
            eng.wait_ge(s_st[n % 2], 128 * (n // 2 + 1))

        def cols(u):
            return slice((u % NCH) * CH, (u % NCH + 1) * CH)

        block = ctx.enter_context(nc.Block())

        @block.sync
        def _(e):
            for dst, src in ((self_[:, :, :], a["sel"]), (W3[:, :, :], a["W3"]), (W2[:, :, :], a["W2"]),
                             (R[:, :], a["R"]), (alpha[:, :], a["alpha"]), (bias[:, :], a["bias"]),
                             (be3[:, :, :].rearrange("p m c -> p (m c)"), a["be3"].partition_broadcast(128)),
                             (be2[:, :, :].rearrange("p m c -> p (m c)"), a["be2"].partition_broadcast(128))):
                e.dma_start(dst, src).then_inc(s_c, 16)

            def load(n):
                b = n % 2
                if n >= 2:
                    e.wait_ge(g_l, NCH * (n - 1))
                    e.wait_ge(v_y, NCH * (n - 1))
                else:
                    e.wait_ge(s_ms, 2)
                for h in range(2):
                    e.dma_start(X2[b][64 * h:64 * h + 64, :], x[n]).then_inc(s_ld[b], 16)
                for m in range(4):
                    e.dma_start(X4[b][32 * m:32 * m + 16, :], x[n, 16 * m:16 * m + 16]).then_inc(s_ld[b], 16)

            load(0)
            if n_img > 1:
                load(1)
            for n in range(n_img):
                e.wait_ge(v_y, NCH * (n + 1))
                for m in range(4):
                    e.dma_start(yd[n, 16 * m:16 * m + 16], YO[n % 2][32 * m:32 * m + 16, :])\
                     .then_inc(s_st[n % 2], 16)
                if n + 2 < n_img:
                    load(n + 2)
                e.wait_ge(a_hy, NCH * (n + 1))
                e.wait_ge(g_ly, NCH * (n + 1))
                for part, t in enumerate((HO, LO)):
                    for m in range(2):
                        e.dma_start(hld[n, part, 16 * m:16 * m + 16], t[32 * m:32 * m + 16, :].bitcast(F32))\
                         .then_inc(s_st[n % 2], 16)
            for n in range(max(0, n_img - 2), n_img):
                stored(e, n)

        def low_y(e, u):
            n = u // NCH
            e.wait_ge(a_hy, u + 1)
            if u % NCH == 0 and n >= 1:
                stored(e, n - 1)
            e.tensor_tensor(LO[:, cols(u)], YO[n % 2][0:64, cols(u)], HO[:, cols(u)].bitcast(F32),
                            ALU.subtract).then_inc(g_ly, 1)

        @block.gpsimd
        def _(e):
            for i in range(2):
                e.memset(X4[i][:, :], 0.0).then_inc(s_ms, 1)

            def low_x(u):
                e.wait_ge(a_h, u + 1)
                e.tensor_tensor(XX[u % 4][64:128, :], X2[(u // NCH) % 2][64:128, cols(u)],
                                XX[u % 4][64:128, :].bitcast(F32), ALU.subtract).then_inc(g_l, 1)

            low_x(0)
            low_x(1)
            for u in range(NU):
                if u + 2 < NU:
                    low_x(u + 2)
                if u >= 1:
                    low_y(e, u - 1)
            low_y(e, NU - 1)

        @block.scalar
        def _(e):
            def high_x(u):
                if u % NCH == 0:
                    loaded(e, u // NCH)
                if u >= 4:
                    e.wait_ge(p_ab, 4 * (u - 3))
                e.activation(XX[u % 4][:, :], X2[(u // NCH) % 2][:, cols(u)], ACT.Copy).then_inc(a_h, 1)

            def high_y(u):
                n = u // NCH
                e.wait_ge(v_y, u + 1)
                if u % NCH == 0 and n >= 1:
                    stored(e, n - 1)
                e.activation(HO[:, cols(u)], YO[n % 2][0:64, cols(u)], ACT.Copy).then_inc(a_hy, 1)

            high_x(0)
            high_x(1)
            for q in range(NQ):
                u = q // 4
                e.wait_ge(p_ab, q + 1)
                if q >= 4:
                    e.wait_ge(v_u, q - 3)
                e.activation(XB[q % 4][:, :], B[q % 2][:, 0:CH], ACT.Copy).then_inc(a_xb, 1)
                if q % 4 == 1 and u + 2 < NU:
                    high_x(u + 2)
                if q % 4 == 3 and u >= 2:
                    high_y(u - 2)
            for u in range(max(0, NU - 2), NU):
                high_y(u)

        @block.vector
        def _(e):
            k = [0]

            def link(ins):
                ins.then_inc(v_w, 1)
                k[0] += 1
                e.wait_ge(v_w, k[0])

            e.wait_ge(s_c, 16 * 8)
            link(e.tensor_copy(sel[:, :, :], self_[:, :, :]))
            link(e.tensor_tensor(W3[:, :, :], W3[:, :, :], be3[:, :, :], ALU.mult))
            link(e.tensor_scalar(W3[:, :, :], W3[:, :, :], 0.1, None, ALU.mult))
            link(e.tensor_tensor(W2[:, :, :], W2[:, :, :], be2[:, :, :], ALU.mult))
            link(e.tensor_tensor(W3[:, :, :], W3[:, :, :], W2[:, :, :], ALU.add))
            link(e.tensor_tensor(bt[:, 0:1], bias[:, 2:3], bias[:, 3:4], ALU.mult))
            link(e.tensor_scalar(bt[:, 1:2], bt[:, 0:1], 0.1, None, ALU.mult))
            link(e.tensor_tensor(bt[:, 2:3], bias[:, 0:1], bias[:, 1:2], ALU.mult))
            link(e.tensor_tensor(bt[:, 0:1], bt[:, 1:2], bt[:, 2:3], ALU.add))
            e.tensor_copy(bt[:, 1:2], bt[:, 0:1]).then_inc(v_wt, 1)
            e.wait_ge(v_wt, 1)

            def pairs(q):
                e.wait_ge(a_xb, q + 1)
                if q >= 2:
                    e.wait_ge(p_t, q - 1)
                e.scalar_tensor_tensor(out=P2[q % 2][:, :], in0=A[q % 2][:, 0:CH], scalar=alpha[:, 0:1],
                                       in1=XB[q % 4][:, :], op0=ALU.add, op1=ALU.mult).then_inc(v_p2, 1)

            def outer(q):
                e.wait_ge(p_t, q + 1)
                if q >= 2:
                    e.wait_ge(p_r, q - 1)
                e.tensor_tensor(U[q % 2][:, :], T[q % 2][:, 0:CH], XB[q % 4][:, :], ALU.mult).then_inc(v_u, 1)

            def close(u):
                n = u // NCH
                e.wait_ge(p_r, 4 * u + 4)
                if u % NCH == 0:
                    loaded(e, n)
                    if n >= 2:
                        stored(e, n - 2)
                        e.wait_ge(a_hy, NCH * (n - 1))
                        e.wait_ge(g_ly, NCH * (n - 1))
                e.scalar_tensor_tensor(out=YO[n % 2][:, cols(u)], in0=Y[u % 2][:, 0:CH], scalar=bt[:, 0:1],
                                       in1=X4[n % 2][:, cols(u)], op0=ALU.add, op1=ALU.add).then_inc(v_y, 1)

            for i in range(NQ + 6):
                if i < NQ:
                    pairs(i)
                if 0 <= i - 2 < NQ:
                    outer(i - 2)
                if i >= 8 and (i - 8) % 4 == 0 and (i - 8) // 4 < NU:
                    close((i - 8) // 4)
            for u in range((NQ + 5 - 8) // 4 + 1, NU):
                close(u)

        @block.tensor
        def _(e):
            for i in range(NQ + 4):
                if i < NQ:
                    q, u, m = i, i // 4, i % 4
                    if q == 0:
                        e.wait_ge(v_wt, 1)
                    if m == 0:
                        e.wait_ge(g_l, u + 1)
                    if q >= 2:
                        e.wait_ge(v_p2, q - 1)
                        e.wait_ge(a_xb, q - 1)
                    e.matmul(A[q % 2][:, 0:CH], sel[:, m, :], XX[u % 4][:, :], start=True, stop=True)
                    e.matmul(B[q % 2][:, 0:CH], sel[:, 4 + m, :], XX[u % 4][:, :], start=True, stop=True)\
                     .then_inc(p_ab, 1)
                q = i - 1
                if 0 <= q < NQ:
                    e.wait_ge(v_p2, q + 1)
                    if q >= 2:
                        e.wait_ge(v_u, q - 1)
                    e.matmul(T[q % 2][:, 0:CH], W3[:, q % 4, :], P2[q % 2][:, :], start=True, stop=True)\
                     .then_inc(p_t, 1)
                q = i - 3
                if 0 <= q < NQ:
                    u, m = q // 4, q % 4
                    e.wait_ge(v_u, q + 1)
                    if m == 0 and u >= 2:
                        e.wait_ge(v_y, u - 1)
                    e.matmul(Y[u % 2][32 * m:32 * m + 32, 0:CH], R[:, :], U[q % 2][:, :], start=True, stop=True)\
                     .then_inc(p_r, 1)


def attention(nc, a, yd, hld, out, n_img):
    steps, fills, ended, s_end = plan(n_img, 4500)
    total = NT * n_img
    index = {(f.kind, f.n, f.i, f.j): k for k, f in enumerate(fills)}
    ends = {}
    for k, s in ended.items():
        ends.setdefault(s, []).append(k)
    for n in range(n_img):
        for b, r in enumerate(BATCHES):
            assert ended[index["r", n, b, 0]] < NT * n + r[0]
            assert ended[index["g", n, b, 0]] < NT * n + 1
    for s in range(RING, total):
        n, t = divmod(s - RING, NT)
        assert ended[index["z", n, group_of(t), 1]] <= s

    ctx = ExitStack()
    with ctx:
        def sb(name, shape, dt=F32):
            return ctx.enter_context(nc.sbuf_tensor("at_" + name, shape, dt))

        def sem(name):
            return ctx.enter_context(nc.semaphore("at_" + name))

        ring = sb("ring", [128, RING, HW])
        THM = [sb(f"THM{i}", [128, HW], F32R) for i in range(2)]
        THS = sb("THS", [128, HW], F32R)
        YT = [sb(f"YT{i}", [65, 896]) for i in range(2)]
        GT = [sb(f"GT{i}", [128, NT, C]) for i in range(2)]
        SREM = sb("SREM", [128, 2, 7, REM])
        ACC = sb("ACC", [128, 4, QC])
        ZACC = sb("ZACC", [128, 2, QC])
        OUTB = sb("OUTB", [128, HW // 2])
        CIN = sb("CIN", [128, 30, 58])
        ZB = sb("ZB", [128, 30, 56])
        TMP = sb("TMP", [128, HW // 2])
        ZC = sb("ZC", [98, 32])
        MX = sb("MX", [128, 2 * NT, 4])
        NM = sb("NM", [128, 4])
        ZS = sb("ZS", [128, 4, 3])
        ZT = sb("ZT", [128, 4])
        RZ = sb("RZ", [128, 4])
        ones = sb("ones", [128, 32])
        WG = sb("WG", [65, C])
        bn1 = sb("bn1", [65, 5, C])
        bn2 = sb("bn2", [128, 5])
        bq = sb("bq", [128, 5])
        w9 = sb("w9", [128, 9])
        PS = ctx.enter_context(nc.psum_tensor("at_S", [128, MAIN], F32))
        AV = [ctx.enter_context(nc.psum_tensor(f"at_AV{i}", [128, 512], F32)) for i in range(2)]
        att = nc.dram_tensor("att", (2, C, HW), F32, kind="Internal").ap()
        zd = nc.dram_tensor("zd", (2, HW), F32, kind="Internal").ap()
        rzd = nc.dram_tensor("rzd", (2, HW), F32, kind="Internal").ap()

        s_c = sem("c")
        s_thm = [sem(f"thm{i}") for i in range(2)]
        s_ths = [sem(f"ths{i}") for i in range(2)]
        s_yt = [sem(f"yt{i}") for i in range(2)]
        s_acc = sem("acc")
        s_zc = sem("zc")
        s_rz = sem("rz")
        s_ep = sem("ep")
        s_out = sem("out")
        g_ms = sem("gms")
        g_w = sem("gw")
        g_done = sem("gdone")
        a_sq = sem("asq")
        v_w = sem("vw")
        v_wt = sem("vwt")
        v_ms = sem("vms")
        v_nm = sem("vnm")
        v_r = sem("vr")
        v_ev = sem("vev")
        v_rc = sem("vrc")
        pe_s = sem("pes")
        pe_f = sem("pef")
        a_p1 = sem("ap1")
        a_p2 = sem("ap2")

        block = ctx.enter_context(nc.Block())

        def ready_at(n):
            return ended[index["z", n, len(GROUPS) - 1, 1]]

        @block.sync
        def _(e):
            for dst, src in ((bn1[:, 0:4, :].rearrange("p a c -> p (a c)"), a["bn1"].partition_broadcast(65)),
                             (bn1[0:64, 4, :], a["wg"]), (bn2[:, 0:4], a["bn2"]), (w9[:, :], a["w9"])):
                e.dma_start(dst, src).then_inc(s_c, 16)
            e.wait_ge(g_ms, 3)

            def thm(n):
                if n >= 2:
                    e.wait_ge(pe_s, 3 * NT * (n - 1))
                for blk in range(4):
                    e.dma_start(THM[n % 2][32 * blk:32 * blk + 32, :].bitcast(F32), hld[n, blk % 2]).then_inc(s_thm[n % 2], 16)

            def ths(n, h):
                lo, hi = (0, HALF) if h == 0 else (HALF, HW)
                if n >= 1:
                    e.wait_ge(pe_s, 3 * (NT * (n - 1) + (12 if h == 0 else NT)))
                for blk in range(4):
                    e.dma_start(THS[32 * blk:32 * blk + 32, lo:hi].bitcast(F32), hld[n, blk // 2, :, lo:hi])\
                     .then_inc(s_ths[h], 16)

            def yt(n, b):
                k = 4 * n + b
                if k >= 2:
                    e.wait_ge(pe_f, index["g", (k - 2) // 4, (k - 2) % 4, 0] + 1)
                r = BATCHES[b]
                lo, hi = 128 * r[0], min(128 * (r[-1] + 1), HW)
                e.dma_start(YT[k % 2][0:64, 0:hi - lo], yd[n, :, lo:hi]).then_inc(s_yt[k % 2], 16)

            def acc_out(n, kind, i):
                e.wait_ge(v_ev, index[kind, n, len(GROUPS) - 1, i] + 1)
                if kind == "o":
                    for h in range(2):
                        q = 2 * i + h
                        e.dma_start(att[n % 2, :, QC * q:QC * q + QC], ACC[64 * h:64 * h + 64, i, :])\
                         .then_inc(s_acc, 16)
                else:
                    for j in range(4):
                        q = 4 * i + j
                        e.dma_start(zd[n % 2, QC * q:QC * q + QC].rearrange("(o q) -> o q", o=1),
                                    ZACC[32 * j:32 * j + 1, i, :]).then_inc(s_acc, 16)

            def z_in(n):
                e.wait_ge(s_acc, 256 * (n + 1))
                e.dma_start(ZC[:, :], zd[n % 2].rearrange("(p f) -> p f", f=32)).then_inc(s_zc, 16)

            def z_out(n):
                e.wait_ge(v_rc, n + 1)
                e.dma_start(rzd[n % 2].rearrange("(p f) -> p f", f=32), ZC[:, :]).then_inc(s_rz, 16)
                e.wait_ge(s_rz, 16 * (n + 1))
                if n >= 1:
                    e.wait_ge(g_done, n)
                    e.wait_ge(s_out, 32 * n)
                for h in range(2):
                    p = slice(64 * h, 64 * h + 64)
                    r0, r1, d0 = (0, 29, 1) if h == 0 else (27, 56, 0)
                    e.dma_start(ZB[p, d0:d0 + 29, :].rearrange("p r w -> p (r w)"),
                                rzd[n % 2, W * r0:W * r1].partition_broadcast(64)).then_inc(s_ep, 16)
                    e.dma_start(CIN[p, d0:d0 + 29, 1:57],
                                att[n % 2, :, W * r0:W * r1].rearrange("c (r w) -> c r w", w=W)).then_inc(s_ep, 16)
                    e.dma_start(OUTB[p, :], yd[n, :, HW // 2 * h:HW // 2 * (h + 1)]).then_inc(s_ep, 16)

            def store(n):
                e.wait_ge(g_done, n + 1)
                for h in range(2):
                    e.dma_start(out[n, :, HW // 2 * h:HW // 2 * (h + 1)], OUTB[64 * h:64 * h + 64, :])\
                     .then_inc(s_out, 16)

            todo = []
            for n in range(n_img):
                f = NT * n
                todo.append((f - NT + 0.2 if n >= 1 else -9, thm, (n,)))
                todo.append((f - NT + 13 if n >= 1 else -8, ths, (n, 0)))
                todo.append((f + 0.1 if n >= 1 else -7, ths, (n, 1)))
                for b in range(4):
                    k = index["g", n, b, 0]
                    todo.append((ended[k] - 5 + 0.01 * b if n >= 1 else -6 + 0.1 * b, yt, (n, b)))
                for kind, m in (("o", 4), ("z", 2)):
                    for i in range(m):
                        todo.append((ended[index[kind, n, len(GROUPS) - 1, i]] + 1, acc_out, (n, kind, i)))
                r = ready_at(n)
                todo.append((r + 1.5, z_in, (n,)))
                todo.append((r + 4, z_out, (n,)))
                todo.append((r + 15, store, (n,)))
            for _, f, args in sorted(todo, key=lambda v: v[0]):
                f(*args)
            e.wait_ge(s_out, 32 * n_img)

        @block.gpsimd
        def _(e):
            for t in (ones,):
                e.memset(t[:, :], 1.0).then_inc(g_ms, 1)
            e.memset(CIN[:, :, :], 0.0).then_inc(g_ms, 1)
            e.memset(ZB[:, :, :], 0.0).then_inc(g_ms, 1)
            k = [0]

            def link(ins):
                ins.then_inc(g_w, 1)
                k[0] += 1
                e.wait_ge(g_w, k[0])

            O3 = OUTB[:, :].rearrange("p (r w) -> p r w", w=W)
            T3 = TMP[:, :].rearrange("p (r w) -> p r w", w=W)
            e.wait_ge(v_wt, 1)
            for n in range(n_img):
                e.wait_ge(s_ep, 96 * (n + 1))
                link(e.tensor_tensor(CIN[:, :, 1:57], CIN[:, :, 1:57], ZB[:, :, :], ALU.mult))
                link(e.tensor_scalar(OUTB[:, :], OUTB[:, :], 1.0, bq[:, 4:5], ALU.mult, ALU.add))
                for i in range(3):
                    for j in range(3):
                        v = 3 * i + j
                        link(e.tensor_scalar(T3, CIN[:, i:i + 28, j:j + 56], w9[:, v:v + 1], 0.0,
                                             ALU.mult, ALU.add))
                        if v < 8:
                            link(e.tensor_tensor(O3, O3, T3, ALU.add))
                        else:
                            e.tensor_tensor(O3, O3, T3, ALU.add).then_inc(g_done, 1)

        @block.scalar
        def _(e):
            e.wait_ge(v_w, 2)
            e.activation(bn1[:, 3, :], bn1[:, 3, :], ACT.Sqrt).then_inc(a_sq, 1)
            e.activation(bn2[:, 3:4], bn2[:, 3:4], ACT.Sqrt).then_inc(a_sq, 1)

            def first(s):
                n, t = divmod(s, NT)
                k, i = KEYS[t], s % 4
                e.wait_ge(v_nm, s + 1)
                if s >= RING:
                    m, u = divmod(s - RING, NT)
                    e.wait_ge(pe_f, index["z", m, group_of(u), 1] + 1)
                b = batch_of(t)
                dst = ring[0:k, s % RING, :]
                for c, (lo, hi, src) in enumerate(((0, 1024, PS[0:k, 0:1024]), (1024, MAIN, PS[0:k, 1024:MAIN]),
                                                   (MAIN, HW, SREM[0:k, b % 2, t - BATCHES[b][0], :]))):
                    e.activation(dst[:, lo:hi], src, ACT.Exp, bias=NM[0:k, i:i + 1],
                                 accum_out=ZS[0:k, i, c:c + 1]).then_inc(a_p1, 1)

            def second(s):
                k, i = KEYS[s % NT], s % 4
                e.wait_ge(v_r, s + 1)
                v = ring[0:k, s % RING, :]
                e.activation(v, v, ACT.Exp, scale=RZ[0:k, i:i + 1]).then_inc(a_p2, 1)

            for s in range(total + 1):
                if s < total:
                    first(s)
                if s >= 1:
                    second(s - 1)

        @block.vector
        def _(e):
            k = [0]

            def link(ins):
                ins.then_inc(v_w, 1)
                k[0] += 1
                e.wait_ge(v_w, k[0])

            for i in range(2):
                e.memset(YT[i][64:65, :], 1.0).then_inc(v_ms, 1)
            e.wait_ge(s_c, 16 * 4)
            link(e.tensor_scalar(bn1[:, 3, :], bn1[:, 3, :], EPS, None, ALU.add))
            link(e.tensor_scalar(bn2[:, 3:4], bn2[:, 3:4], EPS, None, ALU.add))
            e.wait_ge(a_sq, 2)
            link(e.reciprocal(bn1[:, 3, :], bn1[:, 3, :]))
            link(e.tensor_tensor(bn1[:, 0, :], bn1[:, 0, :], bn1[:, 3, :], ALU.mult))
            link(e.tensor_tensor(bn1[:, 2, :], bn1[:, 2, :], bn1[:, 0, :], ALU.mult))
            link(e.tensor_tensor(WG[0:64, :], bn1[0:64, 4, :], bn1[0:64, 0, :], ALU.mult))
            link(e.tensor_tensor(WG[64:65, :], bn1[64:65, 1, :], bn1[64:65, 2, :], ALU.subtract))
            link(e.reciprocal(bq[:, 0:1], bn2[:, 3:4]))
            link(e.tensor_tensor(bq[:, 1:2], bn2[:, 0:1], bq[:, 0:1], ALU.mult))
            link(e.tensor_tensor(bq[:, 2:3], bn2[:, 2:3], bq[:, 1:2], ALU.mult))
            link(e.tensor_tensor(bq[:, 4:5], bn2[:, 1:2], bq[:, 2:3], ALU.subtract))
            e.tensor_scalar(w9[:, :], w9[:, :], bq[:, 1:2], float(W) / float(H), ALU.mult, ALU.mult)\
             .then_inc(v_wt, 1)

            def negmax(s):
                n, t = divmod(s, NT)
                r, i = KEYS[t], s % (2 * NT)
                for c in range(3):
                    e.wait_ge(pe_s, 3 * s + c + 1)
                    ins = e.tensor_reduce(MX[0:r, i, c:c + 1], PS[0:r, 1024 * c:1024 * c + 1024], axis=AX.X,
                                          op=ALU.max)
                link(ins)
                if s >= 4:
                    e.wait_ge(a_p1, 3 * (s - 3))
                e.tensor_reduce(NM[0:r, s % 4:s % 4 + 1], MX[0:r, i, :], axis=AX.X, op=ALU.max, negate=True)\
                 .then_inc(v_nm, 1)

            def recip(s):
                r, i = KEYS[s % NT], s % 4
                e.wait_ge(a_p1, 3 * (s + 1))
                if s >= 4:
                    e.wait_ge(a_p2, s - 3)
                link(e.tensor_reduce(ZT[0:r, i:i + 1], ZS[0:r, i, :], axis=AX.X, op=ALU.add))
                e.reciprocal(RZ[0:r, i:i + 1], ZT[0:r, i:i + 1]).then_inc(v_r, 1)

            def evacuate(f):
                fl, src = fills[f], AV[f % 2]
                e.wait_ge(pe_f, f + 1)
                if fl.kind in "gr":
                    r = BATCHES[fl.i]
                    full = [t for t in r if KEYS[t] == 128]
                    spans = [(128, full[0], len(full))] + [(KEYS[t], t, 1) for t in r if KEYS[t] != 128]
                    for p, t0, m in spans:
                        o = t0 - r[0]
                        v = src[0:p, 64 * o:64 * (o + m)].rearrange("p (t c) -> p t c", c=64)
                        if fl.kind == "g":
                            ins = e.tensor_scalar(GT[fl.n % 2][0:p, t0:t0 + m, :], v, 0.0, 6.0, ALU.max, ALU.min)
                        else:
                            prev = 4 * fl.n + fl.i - 2
                            if prev >= 0:
                                pn, pb = divmod(prev, 4)
                                e.wait_ge(a_p1, 3 * (NT * pn + BATCHES[pb][-1] + 1))
                            e.tensor_copy(SREM[0:p, fl.i % 2, o:o + m, :], v)
                            i0 = NT * (fl.n % 2) + t0
                            ins = e.tensor_reduce(MX[0:p, i0:i0 + m, 3:4], v, axis=AX.X, op=ALU.max)
                elif fl.kind == "o":
                    v = ACC[:, fl.j, :]
                    if fl.i == 0:
                        if fl.n >= 1:
                            e.wait_ge(s_acc, 256 * fl.n)
                        ins = e.tensor_copy(v, src[:, 0:QC])
                    else:
                        ins = e.tensor_tensor(v, src[:, 0:QC], v, ALU.add)
                else:
                    v = ZACC[:, fl.j, :]
                    if fl.i == 0:
                        if fl.n >= 1:
                            e.wait_ge(s_acc, 256 * fl.n)
                        ins = e.tensor_copy(v, src[:, 0:QC])
                    else:
                        ins = e.tensor_tensor(v, src[:, 0:QC], v, ALU.add)
                ins.then_inc(v_ev, 1)

            rc = {ready_at(n) + 3: n for n in range(n_img)}
            for s in range(-3, s_end + 5):
                if 0 <= s < total:
                    negmax(s)
                if 1 <= s <= total:
                    recip(s - 1)
                for f in ends.get(s, []):
                    evacuate(f)
                if s in rc:
                    n = rc[s]
                    e.wait_ge(s_zc, 16 * (n + 1))
                    e.reciprocal(ZC[:, :], ZC[:, :]).then_inc(v_rc, 1)

        @block.tensor
        def _(e):
            def scores(s):
                n, t = divmod(s, NT)
                r = KEYS[t]
                if t == 0:
                    e.wait_ge(s_thm[n % 2], 64 * (n // 2 + 1))
                    e.wait_ge(s_ths[0], 64 * (n + 1))
                if t == 12:
                    e.wait_ge(s_ths[1], 64 * (n + 1))
                lhs = THS[:, 128 * t:128 * t + r]
                for c in range(3):
                    if s >= 1 and c < 2:
                        e.wait_ge(a_p1, 3 * (s - 1) + c + 1)
                    for h in range(2):
                        q = 1024 * c + 512 * h
                        ins = e.matmul(PS[0:r, q:q + 512], lhs, THM[n % 2][:, q:q + 512], start=True, stop=True)
                    ins.then_inc(pe_s, 1)

            def op(f, i):
                fl = fills[f]
                dst = AV[f % 2]
                t, j = fl.ops[i]
                r = KEYS[t]
                if i == 0:
                    if f >= 2:
                        e.wait_ge(v_ev, f - 1)
                    if fl.kind == "g":
                        if fl.n == 0 and fl.i == 0:
                            e.wait_ge(v_wt, 1)
                        k = 4 * fl.n + fl.i
                        e.wait_ge(s_yt[k % 2], 16 * (k // 2 + 1))
                    elif fl.kind == "r":
                        e.wait_ge(s_thm[fl.n % 2], 64 * (fl.n // 2 + 1))
                        e.wait_ge(s_ths[0], 64 * (fl.n + 1))
                        if fl.i >= 1:
                            e.wait_ge(s_ths[1], 64 * (fl.n + 1))
                    else:
                        e.wait_ge(a_p2, NT * fl.n + GROUPS[fl.i][-1] + 1)
                        e.wait_ge(v_ev, index["g", fl.n, 3, 0] + 1)
                o = t - BATCHES[fl.i][0] if fl.kind in "gr" else 0
                slot = (NT * fl.n + t) % RING
                if fl.kind == "g":
                    ins = e.matmul(dst[0:r, 64 * o:64 * o + 64], YT[(4 * fl.n + fl.i) % 2][:, 128 * o:128 * o + r],
                                   WG[:, :], start=True, stop=True)
                elif fl.kind == "r":
                    ins = e.matmul(dst[0:r, 64 * o:64 * o + 64], THS[:, 128 * t:128 * t + r],
                                   THM[fl.n % 2][:, MAIN:HW], start=True, stop=True)
                elif fl.kind == "o":
                    q = QC * (2 * fl.j + j)
                    ins = e.matmul(dst[64 * j:64 * j + 64, 0:QC], GT[fl.n % 2][0:r, t, :], ring[0:r, slot, q:q + QC],
                                   start=(t == GROUPS[fl.i][0]), stop=(t == GROUPS[fl.i][-1]))
                else:
                    q = QC * (4 * fl.j + j)
                    ins = e.matmul(dst[32 * j:32 * j + 32, 0:QC], ones[0:r, :], ring[0:r, slot, q:q + QC],
                                   start=(t == GROUPS[fl.i][0]), stop=(t == GROUPS[fl.i][-1]))
                if i == len(fl.ops) - 1:
                    ins.then_inc(pe_f, 1)

            e.wait_ge(g_ms, 3)
            e.wait_ge(v_ms, 2)
            for s in range(-3, s_end):
                if 0 <= s < total:
                    scores(s)
                for f, i in steps.get(s, []):
                    op(f, i)


def tables():
    sel = np.zeros((128, 8, 128), np.float32)
    alpha = np.zeros((128, 1), np.float32)
    red = np.zeros((128, 32), np.float32)
    linear = {7: (0, 7), 0: (6, 0), **{b: (7, b) for b in range(1, 7)}}
    pair = {(a_, b): ((7, 0) if (a_, b) == (0, 7) else (a_, b)) for a_ in range(8) for b in range(a_, 8)}
    for gg in range(2):
        for row in linear.values():
            alpha[64 * gg + 8 * row[0] + row[1]] = 1.0
        for o in range(8):
            red[64 * gg + 8 * o:64 * gg + 8 * o + 8, 8 * gg + o] = 1.0
    for m in range(4):
        for gg in range(2):
            c0 = 16 * m + 8 * gg
            for ra, rb in pair.values():
                col = 64 * gg + 8 * ra + rb
                for part in range(2):
                    sel[64 * part + c0 + ra, m, col] = 1.0
            for ra in range(8):
                for rb in range(8):
                    for part in range(2):
                        sel[64 * part + c0 + rb, 4 + m, 64 * gg + 8 * ra + rb] = 1.0
    return sel, alpha, red, linear, pair


def lay_out(inputs):
    f = np.float32
    sel, alpha, red, linear, pair = tables()
    W2, W3 = np.asarray(inputs["L0_conv_W2"]), np.asarray(inputs["L0_conv_W3"])
    t3 = [(i, j, k) for i in range(8) for j in range(i, 8) for k in range(j, 8)]
    t2 = [(i, j) for i in range(8) for j in range(i, 8)]
    w3, w2 = np.zeros((128, 4, 128), f), np.zeros((128, 4, 128), f)
    for g in range(8):
        m, gg = divmod(g, 2)
        for o in range(8):
            for c, (i, j, k) in enumerate(t3):
                ra, rb = pair[j, k]
                w3[64 * gg + 8 * ra + rb, m, 64 * gg + 8 * o + i] = W3[g, o, c]
            for c, (i, j) in enumerate(t2):
                ra, rb = linear[j]
                w2[64 * gg + 8 * ra + rb, m, 64 * gg + 8 * o + i] = W2[g, o, c]

    def gapped(v):
        return np.concatenate([np.asarray(v).reshape(4, 16), np.zeros((4, 16), f)], 1).reshape(128)

    beta2, beta3 = (np.asarray(inputs[k]).reshape(C) for k in ("L0_conv_beta2", "L0_conv_beta3"))
    bias = np.stack([gapped(inputs["L0_conv_b2"]), gapped(beta2), gapped(inputs["L0_conv_b3"]), gapped(beta3)], 1)
    vec = {k: np.asarray(inputs["L1_conv_" + k]) for k in
           ("gamma1", "beta1", "mean1", "var1", "gamma2", "beta2", "mean2", "var2")}
    bn2 = np.stack([np.tile(vec[k], 2) for k in ("gamma2", "beta2", "mean2", "var2")], 1)
    w9 = np.asarray(inputs["L1_conv_w_dw"]).reshape(C, 9)
    return {
        "x": np.asarray(inputs["x"]),
        "sel": sel, "alpha": alpha, "R": red, "W3": w3, "W2": w2,
        "be3": np.repeat(beta3, 8), "be2": np.repeat(beta2, 8), "bias": bias,
        "bn1": np.concatenate([vec[k] for k in ("gamma1", "beta1", "mean1", "var1")]),
        "wg": np.asarray(inputs["L1_conv_w_inside"]).reshape(C, C).T,
        "bn2": bn2, "w9": np.concatenate([w9, w9], 0),
    }


def program(nc, arrays):
    a = {}
    for name, v in arrays.items():
        a[name] = nc.dram_tensor(f"in_{name}", v.shape, mybir.dt.from_np(v.dtype), kind="ExternalInput").ap()
    n_img = arrays["x"].shape[0]
    out = nc.dram_tensor("out_0", (n_img, C, H, W), F32, kind="ExternalOutput").ap()
    build(nc, a, out, n_img)


def kernel(**inputs):
    import concourse.bacc as bacc
    from concourse.bass_utils import run_bass_kernel_spmd

    arrays = {k: np.ascontiguousarray(v) for k, v in lay_out(inputs).items()}
    nc = bacc.Bacc("TRN2", target_bir_lowering=False, num_devices=1, dynamic_dma_scratch_size=1024)
    program(nc, arrays)
    r = run_bass_kernel_spmd(nc, [{f"in_{k}": v for k, v in arrays.items()}], core_ids=[0])
    return r.results[0]["out_0"]
```

```python
from contextlib import ExitStack

import numpy as np

import concourse.bass as bass
import concourse.mybir as mybir

F32 = mybir.dt.float32
F32R = mybir.dt.float32r
ALU = mybir.AluOpType
ACT = mybir.ActivationFunctionType
AX = mybir.AxisListType

C, H, W = 64, 56, 56
HW = H * W
G, CPG = 8, 8
EPS = 1e-5

NCH = 7
LAG_T, LAG_U, LAG_R, LAG_Y = 2, 2, 5, 5
CH = HW // NCH

NT = 25
KEYS = [128] * 24 + [64]
MAIN = 3072
PIECE = MAIN // 2
LAT = 60
HOLD = 300
MAXES = ((0, 512), (512, 1536), (1536, 2048), (2048, 3072))
REM = HW - MAIN
GROUPS = [range(a, b) for a, b in ((0, 4), (4, 8), (8, 12), (12, 16), (16, 19), (19, 22), (22, 25))]
BATCHES = [range(0, 7), range(7, 13), range(13, 19), range(19, 25)]
RING = 10
QC = 392
HALF = 1536


def group_of(t):
    return next(g for g, r in enumerate(GROUPS) if t in r)


def batch_of(t):
    return next(b for b, r in enumerate(BATCHES) if t in r)


class Fill:

    def __init__(self, kind, n, i, j, first, last):
        self.kind, self.n, self.i, self.j, self.first, self.last = kind, n, i, j, first, last
        tiles = BATCHES[i] if kind in "gr" else GROUPS[i]
        width = {"g": 1, "r": 1, "o": 2, "z": 4}[kind]
        self.units = [[(t, h) for h in range(width)] for t in tiles]
        self.cost = {"g": 115, "r": 110, "o": 700, "z": 720}[kind]
        self.clear = {"g": 560, "r": 1100, "o": 520, "z": 520}[kind]


def plan(n_img):
    total = NT * n_img
    pre, main = [], []
    for n in range(n_img):
        for b, r in enumerate(BATCHES):
            f = NT * n + r[0]
            pre.append(Fill("r", n, b, 0, f - 5 if f else -1, f - 2 if f else -1))
            f = NT * (n - 1) + 8 + 4 * b
            pre.append(Fill("g", n, b, 0, f if n else -1, f + 3 if n else -1))
        for g, r in enumerate(GROUPS):
            first = NT * n + r[-1]
            main += [Fill("o", n, g, p, first, 0) for p in range(4)]
            main += [Fill("z", n, g, i, first, 0) for i in range(2)]
    pre.sort(key=lambda f: (f.last, f.kind == "g"))
    inf = float("inf")
    fills, ended, cleared = [], {}, {}
    pe, dve = [], []
    end_s, end_a, end_p2, end_m, end_r = {}, {}, {}, {}, {}
    group_end, rests = {}, {}
    tp = ta = td = 0.0
    n_s = n_a = n_m = n_r = n_ev = 0
    cur, at, t_fill = None, 0, {}
    while pre or main or cur or n_r < total or n_ev < len(fills):
        cand = []
        if n_s < 2 * total:
            s, h = divmod(n_s, 2)
            t = 0 if s == 0 else end_a.get((s - 1, h), inf) + LAT
            cand.append((tp if tp < t <= tp + HOLD else max(tp, t), 0, "S"))
        s_now = (n_s + 1) // 2
        if cur is not None:
            f = fills[cur]
            cand.append((max(tp, t_fill[cur]), 1, "op"))
        else:
            k = len(fills)
            free = -inf if k < 2 else cleared.get(k - 2, inf) + LAT
            pick = None
            if pre and pre[0].last < s_now:
                pick = pre
            elif main and max(end_p2.get(main[0].first, inf) + LAT, free) <= tp:
                pick = main
            elif pre and pre[0].first < s_now:
                pick = pre
            elif main:
                pick = main
            if pick:
                f = pick[0]
                t = max(tp, free, 0 if f.kind in "gr" else end_p2.get(f.first, inf) + LAT)
                cand.append((t, 1, "new"))
        best_p = min(cand) if cand else (inf, 9, "")
        if n_a < total * 2 + 1:
            s, part = divmod(n_a, 2)
            if part == 0 and s < total:
                free = 0.0
                if s >= RING:
                    m, u = divmod(s - RING, NT)
                    free = group_end.get((m, group_of(u)), inf) + LAT
                t_a = max(ta, end_m.get(s, inf) + LAT, free)
            elif part == 0:
                t_a = ta
            else:
                t_a = ta if s == 0 else max(ta, end_r.get(s - 1, inf) + LAT)
        else:
            t_a = inf
        cv = []
        if n_m < 5 * total:
            s, part = divmod(n_m, 5)
            if part < 4:
                cv.append((max(td, end_s.get((s, part), inf) + LAT), 1, "M"))
            else:
                cv.append((max(td, end_m[s, 3] + 120, rests.get((s // NT, batch_of(s % NT)), inf)), 0, "nm"))
        if n_r < total and n_m % 5 != 4:
            cv.append((max(td, end_a.get((n_r, 2), inf) + LAT), 2, "r"))
        if n_ev < len(fills) and n_ev in ended:
            t = max(td, t_fill[n_ev] + LAT)
            s, part = divmod(n_m, 5)
            work = [4000, 3400, 2300, 1700, 200][part]
            slack = part != 4 and max(t, td) + fills[n_ev].clear + work < ta
            cv.append((t, 0.5 if slack else 3, "ev"))
        best_v = min(cv) if cv else (inf, 9, "")
        if min(best_p[0], t_a, best_v[0]) == inf:
            raise ValueError("the plan is stuck")
        if t_a <= best_p[0] and t_a <= best_v[0]:
            s, part = divmod(n_a, 2)
            if part == 0 and s < total:
                end_a[s, 0] = t_a + 1420
                end_a[s, 1] = t_a + 1510 + 1420
                end_a[s, 2] = ta = t_a + 3020 + 240
            elif part == 1 and s >= 1:
                end_p2[s - 1] = ta = t_a + 2800
            n_a += 1
            if n_a == 2 * total:
                n_a += 1
                end_p2[total - 1] = ta = max(ta, end_r.get(total - 1, ta)) + 2800
        elif best_p[0] <= best_v[0]:
            t, _, what = best_p
            if what == "S":
                s, h = divmod(n_s, 2)
                if s:
                    t = max(t, end_a[s - 1, h] + LAT)
                tp = end_s[s, 2 * h + 1] = t + 700
                end_s[s, 2 * h] = t + 220
                pe.append(("S", s, h))
                n_s += 1
            else:
                if what == "new":
                    fills.append(pick.pop(0))
                    cur, at = len(fills) - 1, 0
                f = fills[cur]
                pe.append(("op", cur, at))
                t_fill[cur] = tp = t + f.cost
                at += 1
                if at == len(f.units):
                    ended[cur] = (n_s - 1) // 2
                    if f.kind == "z" and f.j == 1:
                        group_end[f.n, f.i] = tp
                    cur = None
        else:
            t, _, what = best_v
            if what == "M":
                s, part = divmod(n_m, 5)
                td = end_m[s, part] = t + (600, 1135)[part % 2]
                dve.append(("M", s, part))
                n_m += 1
            elif what == "nm":
                s = n_m // 5
                td = end_m[s] = t + 70
                dve.append(("nm", s))
                n_m += 1
            elif what == "r":
                td = end_r[n_r] = t + 550
                dve.append(("r", n_r))
                n_r += 1
            else:
                td = cleared[n_ev] = t + fills[n_ev].clear
                if fills[n_ev].kind == "r":
                    rests[fills[n_ev].n, fills[n_ev].i] = td + 120
                dve.append(("ev", n_ev))
                n_ev += 1
    return pe, dve, fills, ended


def build(nc, a, out, n_img):
    x = a["x"].rearrange("n c h w -> n c (h w)")
    yd = nc.dram_tensor("yd", (n_img, C, HW), F32, kind="Internal").ap()
    hld = nc.dram_tensor("hld", (n_img, 2, 32, HW), F32, kind="Internal").ap()
    layer0(nc, a, x, yd, hld, n_img)
    attention(nc, a, yd, hld, out.rearrange("n c h w -> n c (h w)"), n_img)


def layer0(nc, a, x, yd, hld, n_img):
    ctx = ExitStack()
    with ctx:
        def sb(name, shape, dt=F32):
            return ctx.enter_context(nc.sbuf_tensor("l0_" + name, shape, dt))

        def sem(name):
            return ctx.enter_context(nc.semaphore("l0_" + name))

        X2 = [sb(f"X2{i}", [128, HW]) for i in range(2)]
        X4 = [sb(f"X4{i}", [128, HW]) for i in range(2)]
        YO = [sb(f"YO{i}", [128, HW]) for i in range(2)]
        HO = [sb(f"HO{i}", [64, HW], F32R) for i in range(2)]
        LO = [sb(f"LO{i}", [64, HW], F32R) for i in range(2)]
        XX = [sb(f"XX{i}", [128, CH], F32R) for i in range(4)]
        XB = [sb(f"XB{i}", [128, CH]) for i in range(8)]
        P2 = [sb(f"P2{i}", [128, CH]) for i in range(4)]
        U = [sb(f"U{i}", [128, CH]) for i in range(8)]
        self_ = sb("self", [128, 8, 128])
        sel = sb("sel", [128, 8, 128], F32R)
        R = sb("R", [128, 32])
        alpha = sb("alpha", [128, 1])
        W3 = sb("W3", [128, 4, 128])
        W2 = sb("W2", [128, 4, 128])
        be3 = sb("be3", [128, 4, 128])
        be2 = sb("be2", [128, 4, 128])
        bias = sb("bias", [128, 4])
        bt = sb("bt", [128, 3])
        A = [ctx.enter_context(nc.psum_tensor(f"l0_A{i}", [128, 512], F32)) for i in range(3)]
        B = [ctx.enter_context(nc.psum_tensor(f"l0_B{i}", [128, 512], F32)) for i in range(2)]
        T = [ctx.enter_context(nc.psum_tensor(f"l0_T{i}", [128, 512], F32)) for i in range(2)]
        Y = ctx.enter_context(nc.psum_tensor("l0_Y", [128, 512], F32))

        s_c = sem("c")
        s_ld = [sem(f"ld{i}") for i in range(2)]
        s_st = [sem(f"st{i}") for i in range(2)]
        s_ms = sem("ms")
        v_w = sem("vw")
        v_wt = sem("vwt")
        p_ab = sem("pab")
        p_t = sem("pt")
        p_r = sem("pr")
        a_xb = sem("axb")
        a_h = sem("ah")
        a_hy = sem("ahy")
        g_l = sem("gl")
        g_ly = sem("gly")
        v_p2 = sem("vp2")
        v_u = sem("vu")
        v_y = sem("vy")

        NU = NCH * n_img
        NQ = 4 * NU

        def loaded(eng, n):
            eng.wait_ge(s_ld[n % 2], 96 * (n // 2 + 1))

        def stored(eng, n):
            eng.wait_ge(s_st[n % 2], 128 * (n // 2 + 1))

        def cols(u):
            return slice((u % NCH) * CH, (u % NCH + 1) * CH)

        block = ctx.enter_context(nc.Block())

        @block.sync
        def _(e):
            for dst, src in ((self_[:, :, :], a["sel"]), (W3[:, :, :], a["W3"]), (W2[:, :, :], a["W2"]),
                             (R[:, :], a["R"]), (alpha[:, :], a["alpha"]), (bias[:, :], a["bias"]),
                             (be3[:, :, :].rearrange("p m c -> p (m c)"), a["be3"].partition_broadcast(128)),
                             (be2[:, :, :].rearrange("p m c -> p (m c)"), a["be2"].partition_broadcast(128))):
                e.dma_start(dst, src).then_inc(s_c, 16)

            def load(n):
                b = n % 2
                if n >= 2:
                    e.wait_ge(g_l, NCH * (n - 1))
                    e.wait_ge(v_y, NCH * (n - 1))
                else:
                    e.wait_ge(s_ms, 2)
                for h in range(2):
                    e.dma_start(X2[b][64 * h:64 * h + 64, :], x[n]).then_inc(s_ld[b], 16)
                for m in range(4):
                    e.dma_start(X4[b][32 * m:32 * m + 16, :], x[n, 16 * m:16 * m + 16]).then_inc(s_ld[b], 16)

            load(0)
            if n_img > 1:
                load(1)
            for n in range(n_img):
                e.wait_ge(v_y, NCH * (n + 1))
                for m in range(4):
                    e.dma_start(yd[n, 16 * m:16 * m + 16], YO[n % 2][32 * m:32 * m + 16, :])\
                     .then_inc(s_st[n % 2], 16)
                if n + 2 < n_img:
                    load(n + 2)
                e.wait_ge(a_hy, NCH * (n + 1))
                e.wait_ge(g_ly, NCH * (n + 1))
                for part, t in enumerate((HO[n % 2], LO[n % 2])):
                    for m in range(2):
                        e.dma_start(hld[n, part, 16 * m:16 * m + 16], t[32 * m:32 * m + 16, :].bitcast(F32))\
                         .then_inc(s_st[n % 2], 16)
            for n in range(max(0, n_img - 2), n_img):
                stored(e, n)

        def low_y(e, u):
            n = u // NCH
            e.wait_ge(a_hy, u + 1)
            if u % NCH == 0 and n >= 2:
                stored(e, n - 2)
            e.tensor_tensor(LO[n % 2][:, cols(u)], YO[n % 2][0:64, cols(u)], HO[n % 2][:, cols(u)].bitcast(F32),
                            ALU.subtract).then_inc(g_ly, 1)

        @block.gpsimd
        def _(e):
            for i in range(2):
                e.memset(X4[i][:, :], 0.0).then_inc(s_ms, 1)

            def low_x(u):
                e.wait_ge(a_h, u + 1)
                e.tensor_tensor(XX[u % 4][64:128, :], X2[(u // NCH) % 2][64:128, cols(u)],
                                XX[u % 4][64:128, :].bitcast(F32), ALU.subtract).then_inc(g_l, 1)

            low_x(0)
            low_x(1)
            for u in range(NU):
                if u + 2 < NU:
                    low_x(u + 2)
                if u >= 1:
                    low_y(e, u - 1)
            low_y(e, NU - 1)

        @block.scalar
        def _(e):
            def high_x(u):
                if u % NCH == 0:
                    loaded(e, u // NCH)
                if u >= 4:
                    e.wait_ge(p_ab, 4 * (u - 3))
                e.activation(XX[u % 4][:, :], X2[(u // NCH) % 2][:, cols(u)], ACT.Copy).then_inc(a_h, 1)

            def high_y(u):
                n = u // NCH
                e.wait_ge(v_y, u + 1)
                if u % NCH == 0 and n >= 2:
                    stored(e, n - 2)
                e.activation(HO[n % 2][:, cols(u)], YO[n % 2][0:64, cols(u)], ACT.Copy).then_inc(a_hy, 1)

            high_x(0)
            high_x(1)
            for q in range(NQ):
                u = q // 4
                e.wait_ge(p_ab, q + 1)
                if q >= 8:
                    e.wait_ge(v_u, q - 7)
                e.activation(XB[q % 8][:, :], B[q % 2][:, 0:CH], ACT.Copy).then_inc(a_xb, 1)
                if q % 4 == 1 and u + 2 < NU:
                    high_x(u + 2)
                if q % 4 == 3 and u >= 2:
                    high_y(u - 2)
            for u in range(max(0, NU - 2), NU):
                high_y(u)

        @block.vector
        def _(e):
            k = [0]

            def link(ins):
                ins.then_inc(v_w, 1)
                k[0] += 1
                e.wait_ge(v_w, k[0])

            e.wait_ge(s_c, 16 * 8)
            link(e.tensor_copy(sel[:, :, :], self_[:, :, :]))
            link(e.tensor_tensor(W3[:, :, :], W3[:, :, :], be3[:, :, :], ALU.mult))
            link(e.tensor_scalar(W3[:, :, :], W3[:, :, :], 0.1, None, ALU.mult))
            link(e.tensor_tensor(W2[:, :, :], W2[:, :, :], be2[:, :, :], ALU.mult))
            link(e.tensor_tensor(W3[:, :, :], W3[:, :, :], W2[:, :, :], ALU.add))
            link(e.tensor_tensor(bt[:, 0:1], bias[:, 2:3], bias[:, 3:4], ALU.mult))
            link(e.tensor_scalar(bt[:, 1:2], bt[:, 0:1], 0.1, None, ALU.mult))
            link(e.tensor_tensor(bt[:, 2:3], bias[:, 0:1], bias[:, 1:2], ALU.mult))
            link(e.tensor_tensor(bt[:, 0:1], bt[:, 1:2], bt[:, 2:3], ALU.add))
            e.tensor_copy(bt[:, 1:2], bt[:, 0:1]).then_inc(v_wt, 1)
            e.wait_ge(v_wt, 1)

            def pairs(q):
                e.wait_ge(a_xb, q + 1)
                if q >= 4:
                    e.wait_ge(p_t, q - 3)
                e.scalar_tensor_tensor(out=P2[q % 4][:, :], in0=A[q % 3][:, 0:CH], scalar=alpha[:, 0:1],
                                       in1=XB[q % 8][:, :], op0=ALU.add, op1=ALU.mult).then_inc(v_p2, 1)

            def outer(q):
                e.wait_ge(p_t, q + 1)
                if q >= 8:
                    e.wait_ge(p_r, q // 4 - 1)
                e.tensor_tensor(U[q % 8][:, :], T[q % 2][:, 0:CH], XB[q % 8][:, :], ALU.mult).then_inc(v_u, 1)

            def close(u):
                n = u // NCH
                e.wait_ge(p_r, u + 1)
                if u % NCH == 0:
                    loaded(e, n)
                    if n >= 2:
                        stored(e, n - 2)
                        e.wait_ge(a_hy, NCH * (n - 1))
                        e.wait_ge(g_ly, NCH * (n - 1))
                e.scalar_tensor_tensor(out=YO[n % 2][:, cols(u)], in0=Y[:, 0:CH], scalar=bt[:, 0:1],
                                       in1=X4[n % 2][:, cols(u)], op0=ALU.add, op1=ALU.add).then_inc(v_y, 1)

            for i in range(NQ + LAG_Y):
                if i < NQ:
                    pairs(i)
                if 0 <= i - LAG_U < NQ:
                    outer(i - LAG_U)
                u, m = divmod(i - LAG_Y, 4)
                if m == 3 and 0 <= u < NU:
                    close(u)

        @block.tensor
        def _(e):
            for i in range(NQ + LAG_R):
                if i < NQ:
                    q, u, m = i, i // 4, i % 4
                    if q == 0:
                        e.wait_ge(v_wt, 1)
                    if m == 0:
                        e.wait_ge(g_l, u + 1)
                    if q >= 3:
                        e.wait_ge(v_p2, q - 2)
                    e.matmul(A[q % 3][:, 0:CH], sel[:, m, :], XX[u % 4][:, :], start=True, stop=True)
                    if q >= 2:
                        e.wait_ge(a_xb, q - 1)
                    e.matmul(B[q % 2][:, 0:CH], sel[:, 4 + m, :], XX[u % 4][:, :], start=True, stop=True)\
                     .then_inc(p_ab, 1)
                q = i - LAG_T
                if 0 <= q < NQ:
                    e.wait_ge(v_p2, q + 1)
                    if q >= 2:
                        e.wait_ge(v_u, q - 1)
                    e.matmul(T[q % 2][:, 0:CH], W3[:, q % 4, :], P2[q % 4][:, :], start=True, stop=True)\
                     .then_inc(p_t, 1)
                u, m = divmod(i - LAG_R, 4)
                if m == 3 and 0 <= u < NU:
                    e.wait_ge(v_u, 4 * u + 4)
                    if u >= 1:
                        e.wait_ge(v_y, u)
                    for m in range(4):
                        ins = e.matmul(Y[32 * m:32 * m + 32, 0:CH], R[:, :], U[(4 * u + m) % 8][:, :],
                                       start=True, stop=True)
                    ins.then_inc(p_r, 1)


def attention(nc, a, yd, hld, out, n_img):
    pe_order, dve_order, fills, ended = plan(n_img)
    total = NT * n_img
    index = {(f.kind, f.n, f.i, f.j): k for k, f in enumerate(fills)}

    ctx = ExitStack()
    with ctx:
        def sb(name, shape, dt=F32):
            return ctx.enter_context(nc.sbuf_tensor("at_" + name, shape, dt))

        def sem(name):
            return ctx.enter_context(nc.semaphore("at_" + name))

        ring = sb("ring", [128, RING, HW])
        THM = [sb(f"THM{i}", [128, HW], F32R) for i in range(2)]
        THS = sb("THS", [128, HW], F32R)
        YT = [sb(f"YT{i}", [65, 896]) for i in range(2)]
        GT = [sb(f"GT{i}", [128, NT, C]) for i in range(2)]
        SREM = sb("SREM", [128, 2, 7, REM])
        ACC = sb("ACC", [128, 4, QC])
        ZACC = sb("ZACC", [128, 2, QC])
        OUTB = sb("OUTB", [128, HW // 2])
        CIN = sb("CIN", [128, 30, 58])
        ZB = sb("ZB", [128, 30, 56])
        TMP = sb("TMP", [128, HW // 2])
        ZC = sb("ZC", [98, 32])
        MX = sb("MX", [128, 2 * NT, 5])
        NM = sb("NM", [128, 4])
        ZS = sb("ZS", [128, 4, 3])
        ZT = sb("ZT", [128, 4])
        RZ = sb("RZ", [128, 4])
        ones = sb("ones", [128, 32])
        WG = sb("WG", [65, C])
        bn1 = sb("bn1", [65, 5, C])
        bn2 = sb("bn2", [128, 5])
        bq = sb("bq", [128, 5])
        w9 = sb("w9", [128, 9])
        PS = ctx.enter_context(nc.psum_tensor("at_S", [128, MAIN], F32))
        AV = [ctx.enter_context(nc.psum_tensor(f"at_AV{i}", [128, 512], F32)) for i in range(2)]
        att = nc.dram_tensor("att", (2, C, HW), F32, kind="Internal").ap()
        zd = nc.dram_tensor("zd", (2, HW), F32, kind="Internal").ap()
        rzd = nc.dram_tensor("rzd", (2, HW), F32, kind="Internal").ap()

        s_c = sem("c")
        s_thm = [sem(f"thm{i}") for i in range(2)]
        s_ths = [sem(f"ths{i}") for i in range(2)]
        s_yt = [sem(f"yt{i}") for i in range(2)]
        s_acc = sem("acc")
        s_zc = sem("zc")
        s_rz = sem("rz")
        s_ep = sem("ep")
        s_out = sem("out")
        g_ms = sem("gms")
        g_w = sem("gw")
        g_done = sem("gdone")
        a_sq = sem("asq")
        v_w = sem("vw")
        v_wt = sem("vwt")
        v_ms = sem("vms")
        v_nm = sem("vnm")
        v_fin = sem("vfin")
        v_m = sem("vm")
        v_r = sem("vr")
        v_ev = sem("vev")
        v_rc = sem("vrc")
        pe_s = sem("pes")
        pe_f = sem("pef")
        a_p1 = sem("ap1")
        a_p2 = sem("ap2")

        block = ctx.enter_context(nc.Block())

        def ready_at(n):
            return ended[index["z", n, len(GROUPS) - 1, 1]]

        @block.sync
        def _(e):
            for dst, src in ((bn1[:, 0:4, :].rearrange("p a c -> p (a c)"), a["bn1"].partition_broadcast(65)),
                             (bn1[0:64, 4, :], a["wg"]), (bn2[:, 0:4], a["bn2"]), (w9[:, :], a["w9"])):
                e.dma_start(dst, src).then_inc(s_c, 16)
            e.wait_ge(g_ms, 3)

            def thm(n):
                if n >= 2:
                    e.wait_ge(pe_s, 4 * NT * (n - 1))
                for blk in range(4):
                    e.dma_start(THM[n % 2][32 * blk:32 * blk + 32, :].bitcast(F32), hld[n, blk % 2]).then_inc(s_thm[n % 2], 16)

            def ths(n, h):
                lo, hi = (0, HALF) if h == 0 else (HALF, HW)
                if n >= 1:
                    e.wait_ge(pe_s, 4 * (NT * (n - 1) + (12 if h == 0 else NT)))
                for blk in range(4):
                    e.dma_start(THS[32 * blk:32 * blk + 32, lo:hi].bitcast(F32), hld[n, blk // 2, :, lo:hi])\
                     .then_inc(s_ths[h], 16)

            def yt(n, b):
                k = 4 * n + b
                if k >= 2:
                    e.wait_ge(pe_f, index["g", (k - 2) // 4, (k - 2) % 4, 0] + 1)
                r = BATCHES[b]
                lo, hi = 128 * r[0], min(128 * (r[-1] + 1), HW)
                e.dma_start(YT[k % 2][0:64, 0:hi - lo], yd[n, :, lo:hi]).then_inc(s_yt[k % 2], 16)

            def acc_out(n, kind, i):
                e.wait_ge(v_ev, index[kind, n, len(GROUPS) - 1, i] + 1)
                if kind == "o":
                    for h in range(2):
                        q = 2 * i + h
                        e.dma_start(att[n % 2, :, QC * q:QC * q + QC], ACC[64 * h:64 * h + 64, i, :])\
                         .then_inc(s_acc, 16)
                else:
                    for j in range(4):
                        q = 4 * i + j
                        e.dma_start(zd[n % 2, QC * q:QC * q + QC].rearrange("(o q) -> o q", o=1),
                                    ZACC[32 * j:32 * j + 1, i, :]).then_inc(s_acc, 16)

            def z_in(n):
                e.wait_ge(s_acc, 256 * (n + 1))
                e.dma_start(ZC[:, :], zd[n % 2].rearrange("(p f) -> p f", f=32)).then_inc(s_zc, 16)

            def z_out(n):
                if n >= 1:
                    e.wait_ge(g_done, n)
                    e.wait_ge(s_out, 32 * n)
                halves = [(slice(64 * h, 64 * h + 64), *((0, 29, 1) if h == 0 else (27, 56, 0)), h) for h in range(2)]
                for p, r0, r1, d0, h in halves:
                    e.dma_start(CIN[p, d0:d0 + 29, 1:57],
                                att[n % 2, :, W * r0:W * r1].rearrange("c (r w) -> c r w", w=W)).then_inc(s_ep, 16)
                    e.dma_start(OUTB[p, :], yd[n, :, HW // 2 * h:HW // 2 * (h + 1)]).then_inc(s_ep, 16)
                e.wait_ge(v_rc, n + 1)
                e.dma_start(rzd[n % 2].rearrange("(p f) -> p f", f=32), ZC[:, :]).then_inc(s_rz, 16)
                e.wait_ge(s_rz, 16 * (n + 1))
                for p, r0, r1, d0, h in halves:
                    e.dma_start(ZB[p, d0:d0 + 29, :].rearrange("p r w -> p (r w)"),
                                rzd[n % 2, W * r0:W * r1].partition_broadcast(64)).then_inc(s_ep, 16)

            def store(n):
                if n < n_img - 1:
                    e.wait_ge(g_done, n + 1)
                else:
                    e.wait_ge(v_fin, 1)
                for h in range(2):
                    e.dma_start(out[n, :, HW // 2 * h:HW // 2 * (h + 1)], OUTB[64 * h:64 * h + 64, :])\
                     .then_inc(s_out, 16)

            todo = []
            for n in range(n_img):
                f = NT * n
                todo.append((f - NT + 0.2 if n >= 1 else -9, thm, (n,)))
                todo.append((f - NT + 13 if n >= 1 else -8, ths, (n, 0)))
                todo.append((f + 0.1 if n >= 1 else -7, ths, (n, 1)))
                for b in range(4):
                    k = index["g", n, b, 0]
                    todo.append((ended[k] - 5 + 0.01 * b if n >= 1 else -6 + 0.1 * b, yt, (n, b)))
                for kind, m in (("o", 4), ("z", 2)):
                    for i in range(m):
                        todo.append((ended[index[kind, n, len(GROUPS) - 1, i]] + 1, acc_out, (n, kind, i)))
                r = ready_at(n)
                todo.append((r + 1.5, z_in, (n,)))
                todo.append((r + 4, z_out, (n,)))
                todo.append((r + 15, store, (n,)))
            for _, f, args in sorted(todo, key=lambda v: v[0]):
                f(*args)
            e.wait_ge(s_out, 32 * n_img)

        @block.gpsimd
        def _(e):
            for t in (ones,):
                e.memset(t[:, :], 1.0).then_inc(g_ms, 1)
            e.memset(CIN[:, :, :], 0.0).then_inc(g_ms, 1)
            e.memset(ZB[:, :, :], 0.0).then_inc(g_ms, 1)
            k = [0]

            def link(ins):
                ins.then_inc(g_w, 1)
                k[0] += 1
                e.wait_ge(g_w, k[0])

            O3 = OUTB[:, :].rearrange("p (r w) -> p r w", w=W)
            T3 = TMP[:, :].rearrange("p (r w) -> p r w", w=W)
            e.wait_ge(v_wt, 1)
            for n in range(n_img - 1):
                e.wait_ge(s_ep, 96 * (n + 1))
                link(e.tensor_tensor(CIN[:, :, 1:57], CIN[:, :, 1:57], ZB[:, :, :], ALU.mult))
                link(e.tensor_scalar(OUTB[:, :], OUTB[:, :], 1.0, bq[:, 4:5], ALU.mult, ALU.add))
                for i in range(3):
                    for j in range(3):
                        v = 3 * i + j
                        link(e.tensor_scalar(T3, CIN[:, i:i + 28, j:j + 56], w9[:, v:v + 1], 0.0,
                                             ALU.mult, ALU.add))
                        if v < 8:
                            link(e.tensor_tensor(O3, O3, T3, ALU.add))
                        else:
                            e.tensor_tensor(O3, O3, T3, ALU.add).then_inc(g_done, 1)

        @block.scalar
        def _(e):
            e.wait_ge(v_w, 2)
            e.activation(bn1[:, 3, :], bn1[:, 3, :], ACT.Sqrt).then_inc(a_sq, 1)
            e.activation(bn2[:, 3:4], bn2[:, 3:4], ACT.Sqrt).then_inc(a_sq, 1)

            def first(s):
                n, t = divmod(s, NT)
                k, i = KEYS[t], s % 4
                e.wait_ge(v_nm, s + 1)
                if s >= RING:
                    m, u = divmod(s - RING, NT)
                    e.wait_ge(pe_f, index["z", m, group_of(u), 1] + 1)
                b = batch_of(t)
                dst = ring[0:k, s % RING, :]
                for c, (lo, hi, src) in enumerate(((0, PIECE, PS[0:k, 0:PIECE]), (PIECE, MAIN, PS[0:k, PIECE:MAIN]),
                                                   (MAIN, HW, SREM[0:k, b % 2, t - BATCHES[b][0], :]))):
                    e.activation(dst[:, lo:hi], src, ACT.Exp, bias=NM[0:k, i:i + 1],
                                 accum_out=ZS[0:k, i, c:c + 1] if c < 2 else None).then_inc(a_p1, 1)

            def second(s):
                k, i = KEYS[s % NT], s % 4
                e.wait_ge(v_r, s + 1)
                v = ring[0:k, s % RING, :]
                e.activation(v, v, ACT.Exp, scale=RZ[0:k, i:i + 1]).then_inc(a_p2, 1)

            for s in range(total + 1):
                if s < total:
                    first(s)
                if s >= 1:
                    second(s - 1)

        @block.vector
        def _(e):
            k = [0]

            def link(ins):
                ins.then_inc(v_w, 1)
                k[0] += 1
                e.wait_ge(v_w, k[0])

            for i in range(2):
                e.memset(YT[i][64:65, :], 1.0).then_inc(v_ms, 1)
            e.wait_ge(s_c, 16 * 4)
            link(e.tensor_scalar(bn1[:, 3, :], bn1[:, 3, :], EPS, None, ALU.add))
            link(e.tensor_scalar(bn2[:, 3:4], bn2[:, 3:4], EPS, None, ALU.add))
            e.wait_ge(a_sq, 2)
            link(e.reciprocal(bn1[:, 3, :], bn1[:, 3, :]))
            link(e.tensor_tensor(bn1[:, 0, :], bn1[:, 0, :], bn1[:, 3, :], ALU.mult))
            link(e.tensor_tensor(bn1[:, 2, :], bn1[:, 2, :], bn1[:, 0, :], ALU.mult))
            link(e.tensor_tensor(WG[0:64, :], bn1[0:64, 4, :], bn1[0:64, 0, :], ALU.mult))
            link(e.tensor_tensor(WG[64:65, :], bn1[64:65, 1, :], bn1[64:65, 2, :], ALU.subtract))
            link(e.reciprocal(bq[:, 0:1], bn2[:, 3:4]))
            link(e.tensor_tensor(bq[:, 1:2], bn2[:, 0:1], bq[:, 0:1], ALU.mult))
            link(e.tensor_tensor(bq[:, 2:3], bn2[:, 2:3], bq[:, 1:2], ALU.mult))
            link(e.tensor_tensor(bq[:, 4:5], bn2[:, 1:2], bq[:, 2:3], ALU.subtract))
            e.tensor_scalar(w9[:, :], w9[:, :], bq[:, 1:2], float(W) / float(H), ALU.mult, ALU.mult)\
             .then_inc(v_wt, 1)

            def piecemax(s, c):
                n, t = divmod(s, NT)
                r, i = KEYS[t], s % (2 * NT)
                lo, hi = MAXES[c]
                e.wait_ge(pe_s, 4 * s + c + 1)
                e.tensor_reduce(MX[0:r, i, c:c + 1], PS[0:r, lo:hi], axis=AX.X,
                                op=ALU.max).then_inc(v_m, 1)

            def negmax(s):
                n, t = divmod(s, NT)
                r, i = KEYS[t], s % (2 * NT)
                e.wait_ge(v_m, 4 * s + 4)
                e.wait_ge(v_ev, index["r", n, batch_of(t), 0] + 1)
                if s >= 4:
                    e.wait_ge(a_p1, 3 * (s - 3))
                e.tensor_reduce(NM[0:r, s % 4:s % 4 + 1], MX[0:r, i, :], axis=AX.X, op=ALU.max, negate=True)\
                 .then_inc(v_nm, 1)

            def recip(s):
                r, i = KEYS[s % NT], s % 4
                e.wait_ge(a_p1, 3 * (s + 1))
                if s >= 4:
                    e.wait_ge(a_p2, s - 3)
                link(e.tensor_reduce(ZS[0:r, i, 2:3], ring[0:r, s % RING, MAIN:HW], axis=AX.X, op=ALU.add))
                link(e.tensor_reduce(ZT[0:r, i:i + 1], ZS[0:r, i, :], axis=AX.X, op=ALU.add))
                e.reciprocal(RZ[0:r, i:i + 1], ZT[0:r, i:i + 1]).then_inc(v_r, 1)

            def shares(n):
                e.wait_ge(s_zc, 16 * (n + 1))
                e.reciprocal(ZC[:, :], ZC[:, :]).then_inc(v_rc, 1)

            def finish(n):
                O3 = OUTB[:, :].rearrange("p (r w) -> p r w", w=W)
                e.wait_ge(s_ep, 96 * (n + 1))
                link(e.tensor_tensor(CIN[:, :, 1:57], CIN[:, :, 1:57], ZB[:, :, :], ALU.mult))
                link(e.tensor_scalar(OUTB[:, :], OUTB[:, :], bq[:, 4:5], None, ALU.add))
                for v in range(9):
                    i, j = divmod(v, 3)
                    ins = e.scalar_tensor_tensor(out=O3, in0=CIN[:, i:i + 28, j:j + 56], scalar=w9[:, v:v + 1],
                                                 in1=O3, op0=ALU.mult, op1=ALU.add)
                    if v < 8:
                        link(ins)
                ins.then_inc(v_fin, 1)

            def evacuate(f):
                fl, src = fills[f], AV[f % 2]
                e.wait_ge(pe_f, f + 1)
                if fl.kind in "gr":
                    r = BATCHES[fl.i]
                    full = [t for t in r if KEYS[t] == 128]
                    spans = [(128, full[0], len(full))] + [(KEYS[t], t, 1) for t in r if KEYS[t] != 128]
                    for p, t0, m in spans:
                        o = t0 - r[0]
                        v = src[0:p, 64 * o:64 * (o + m)].rearrange("p (t c) -> p t c", c=64)
                        if fl.kind == "g":
                            ins = e.tensor_scalar(GT[fl.n % 2][0:p, t0:t0 + m, :], v, 0.0, 6.0, ALU.max, ALU.min)
                        else:
                            prev = 4 * fl.n + fl.i - 2
                            if prev >= 0:
                                pn, pb = divmod(prev, 4)
                                e.wait_ge(a_p1, 3 * (NT * pn + BATCHES[pb][-1] + 1))
                            e.tensor_copy(SREM[0:p, fl.i % 2, o:o + m, :], v)
                            i0 = NT * (fl.n % 2) + t0
                            ins = e.tensor_reduce(MX[0:p, i0:i0 + m, 4:5], v, axis=AX.X, op=ALU.max)
                elif fl.kind == "o":
                    v = ACC[:, fl.j, :]
                    if fl.i == 0:
                        if fl.n >= 1:
                            e.wait_ge(s_acc, 256 * fl.n)
                        ins = e.tensor_copy(v, src[:, 0:QC])
                    else:
                        ins = e.tensor_tensor(v, src[:, 0:QC], v, ALU.add)
                else:
                    v = ZACC[:, fl.j, :]
                    if fl.i == 0:
                        if fl.n >= 1:
                            e.wait_ge(s_acc, 256 * fl.n)
                        ins = e.tensor_copy(v, src[:, 0:QC])
                    else:
                        ins = e.tensor_tensor(v, src[:, 0:QC], v, ALU.add)
                ins.then_inc(v_ev, 1)

            acts = {"M": piecemax, "nm": negmax, "r": recip, "ev": evacuate}
            for n in range(n_img):
                late = dve_order.index(("ev", index["z", n, len(GROUPS) - 1, 1])) + 14
                dve_order.insert(late, ("rc", n))
            acts["rc"] = shares
            for what, *args in dve_order:
                acts[what](*args)
            finish(n_img - 1)

        @block.tensor
        def _(e):
            def scores(s, c):
                n, t = divmod(s, NT)
                r = KEYS[t]
                if t == 0 and c == 0:
                    e.wait_ge(s_thm[n % 2], 64 * (n // 2 + 1))
                    e.wait_ge(s_ths[0], 64 * (n + 1))
                if t == 12 and c == 0:
                    e.wait_ge(s_ths[1], 64 * (n + 1))
                lhs = THS[:, 128 * t:128 * t + r]
                if s >= 1:
                    e.wait_ge(a_p1, 3 * (s - 1) + c + 1)
                for q in range(PIECE * c, PIECE * (c + 1), 512):
                    ins = e.matmul(PS[0:r, q:q + 512], lhs, THM[n % 2][:, q:q + 512], start=True, stop=True)
                    if q + 512 in [hi for _, hi in MAXES]:
                        ins.then_inc(pe_s, 1)

            def unit(f, i):
                fl = fills[f]
                dst = AV[f % 2]
                t = fl.units[i][0][0]
                r = KEYS[t]
                if i == 0:
                    if f >= 2:
                        e.wait_ge(v_ev, f - 1)
                    if fl.kind == "g":
                        if fl.n == 0 and fl.i == 0:
                            e.wait_ge(v_wt, 1)
                        k = 4 * fl.n + fl.i
                        e.wait_ge(s_yt[k % 2], 16 * (k // 2 + 1))
                    elif fl.kind == "r":
                        e.wait_ge(s_thm[fl.n % 2], 64 * (fl.n // 2 + 1))
                        e.wait_ge(s_ths[0], 64 * (fl.n + 1))
                        if fl.i >= 1:
                            e.wait_ge(s_ths[1], 64 * (fl.n + 1))
                    else:
                        e.wait_ge(a_p2, NT * fl.n + GROUPS[fl.i][-1] + 1)
                        e.wait_ge(v_ev, index["g", fl.n, 3, 0] + 1)
                o = t - BATCHES[fl.i][0] if fl.kind in "gr" else 0
                slot = (NT * fl.n + t) % RING
                for _, j in fl.units[i]:
                    if fl.kind == "g":
                        ins = e.matmul(dst[0:r, 64 * o:64 * o + 64], YT[(4 * fl.n + fl.i) % 2][:, 128 * o:128 * o + r],
                                       WG[:, :], start=True, stop=True)
                    elif fl.kind == "r":
                        ins = e.matmul(dst[0:r, 64 * o:64 * o + 64], THS[:, 128 * t:128 * t + r],
                                       THM[fl.n % 2][:, MAIN:HW], start=True, stop=True)
                    elif fl.kind == "o":
                        q = QC * (2 * fl.j + j)
                        ins = e.matmul(dst[64 * j:64 * j + 64, 0:QC], GT[fl.n % 2][0:r, t, :], ring[0:r, slot, q:q + QC],
                                       start=(t == GROUPS[fl.i][0]), stop=(t == GROUPS[fl.i][-1]))
                    else:
                        q = QC * (4 * fl.j + j)
                        ins = e.matmul(dst[32 * j:32 * j + 32, 0:QC], ones[0:r, :], ring[0:r, slot, q:q + QC],
                                       start=(t == GROUPS[fl.i][0]), stop=(t == GROUPS[fl.i][-1]))
                if i == len(fl.units) - 1:
                    ins.then_inc(pe_f, 1)

            e.wait_ge(g_ms, 3)
            e.wait_ge(v_ms, 2)
            for what, f, i in pe_order:
                if what == "S":
                    scores(f, i)
                else:
                    unit(f, i)


def tables():
    sel = np.zeros((128, 8, 128), np.float32)
    alpha = np.zeros((128, 1), np.float32)
    red = np.zeros((128, 32), np.float32)
    linear = {7: (0, 7), 0: (6, 0), **{b: (7, b) for b in range(1, 7)}}
    pair = {(a_, b): ((7, 0) if (a_, b) == (0, 7) else (a_, b)) for a_ in range(8) for b in range(a_, 8)}
    for gg in range(2):
        for row in linear.values():
            alpha[64 * gg + 8 * row[0] + row[1]] = 1.0
        for o in range(8):
            red[64 * gg + 8 * o:64 * gg + 8 * o + 8, 8 * gg + o] = 1.0
    for m in range(4):
        for gg in range(2):
            c0 = 16 * m + 8 * gg
            for ra, rb in pair.values():
                col = 64 * gg + 8 * ra + rb
                for part in range(2):
                    sel[64 * part + c0 + ra, m, col] = 1.0
            for ra in range(8):
                for rb in range(8):
                    for part in range(2):
                        sel[64 * part + c0 + rb, 4 + m, 64 * gg + 8 * ra + rb] = 1.0
    return sel, alpha, red, linear, pair


def lay_out(inputs):
    f = np.float32
    sel, alpha, red, linear, pair = tables()
    W2, W3 = np.asarray(inputs["L0_conv_W2"]), np.asarray(inputs["L0_conv_W3"])
    t3 = [(i, j, k) for i in range(8) for j in range(i, 8) for k in range(j, 8)]
    t2 = [(i, j) for i in range(8) for j in range(i, 8)]
    w3, w2 = np.zeros((128, 4, 128), f), np.zeros((128, 4, 128), f)
    for g in range(8):
        m, gg = divmod(g, 2)
        for o in range(8):
            for c, (i, j, k) in enumerate(t3):
                ra, rb = pair[j, k]
                w3[64 * gg + 8 * ra + rb, m, 64 * gg + 8 * o + i] = W3[g, o, c]
            for c, (i, j) in enumerate(t2):
                ra, rb = linear[j]
                w2[64 * gg + 8 * ra + rb, m, 64 * gg + 8 * o + i] = W2[g, o, c]

    def gapped(v):
        return np.concatenate([np.asarray(v).reshape(4, 16), np.zeros((4, 16), f)], 1).reshape(128)

    beta2, beta3 = (np.asarray(inputs[k]).reshape(C) for k in ("L0_conv_beta2", "L0_conv_beta3"))
    bias = np.stack([gapped(inputs["L0_conv_b2"]), gapped(beta2), gapped(inputs["L0_conv_b3"]), gapped(beta3)], 1)
    vec = {k: np.asarray(inputs["L1_conv_" + k]) for k in
           ("gamma1", "beta1", "mean1", "var1", "gamma2", "beta2", "mean2", "var2")}
    bn2 = np.stack([np.tile(vec[k], 2) for k in ("gamma2", "beta2", "mean2", "var2")], 1)
    w9 = np.asarray(inputs["L1_conv_w_dw"]).reshape(C, 9)
    return {
        "x": np.asarray(inputs["x"]),
        "sel": sel, "alpha": alpha, "R": red, "W3": w3, "W2": w2,
        "be3": np.repeat(beta3, 8), "be2": np.repeat(beta2, 8), "bias": bias,
        "bn1": np.concatenate([vec[k] for k in ("gamma1", "beta1", "mean1", "var1")]),
        "wg": np.asarray(inputs["L1_conv_w_inside"]).reshape(C, C).T,
        "bn2": bn2, "w9": np.concatenate([w9, w9], 0),
    }


def program(nc, arrays):
    a = {}
    for name, v in arrays.items():
        a[name] = nc.dram_tensor(f"in_{name}", v.shape, mybir.dt.from_np(v.dtype), kind="ExternalInput").ap()
    n_img = arrays["x"].shape[0]
    out = nc.dram_tensor("out_0", (n_img, C, H, W), F32, kind="ExternalOutput").ap()
    build(nc, a, out, n_img)


def kernel(**inputs):
    import concourse.bacc as bacc
    from concourse.bass_utils import run_bass_kernel_spmd

    arrays = {k: np.ascontiguousarray(v) for k, v in lay_out(inputs).items()}
    nc = bacc.Bacc("TRN2", target_bir_lowering=False, num_devices=1, dynamic_dma_scratch_size=1024)
    program(nc, arrays)
    r = run_bass_kernel_spmd(nc, [{f"in_{k}": v for k, v in arrays.items()}], core_ids=[0])
    return r.results[0]["out_0"]
```
